# Optimizing a Trainium2 kernel written in Bass

```python
import numpy as np
import jax
import jax.numpy as jnp

def _softmax(x, axis=-1):
    return jax.nn.softmax(x, axis=axis)

def _gelu(x):
    return jax.nn.gelu(x, approximate=True)

def _silu(x):
    return jax.nn.silu(x)

def _sigmoid(x):
    return jax.nn.sigmoid(x)

def _layernorm(x, axis=-1, eps=1e-05):
    m = jnp.mean(x, axis=axis, keepdims=True)
    v = jnp.var(x, axis=axis, keepdims=True)
    return (x - m) / jnp.sqrt(v + eps)

def _scatter_add(tgt, idx, src, axis=0):
    return tgt.at[idx].add(src)

def _segment_sum(src, seg, n):
    return jax.ops.segment_sum(src, seg, n)
kernel_name = 'mk_cond_resid_d4_seqx_r2_8e56ab'

def setup_inputs(seed: int=0):
    np.random.seed(seed)
    _w = jnp.asarray

    def _rec_inputs():
        import jax
        import jax.numpy as jnp
        _rk = jax.random.key(seed)
        x = -0.000125 + 0.9999 * jax.random.normal(jax.random.fold_in(_rk, 1), (2, 2048, 512), jnp.float32)
        _lenS = 2048 - jax.random.randint(jax.random.fold_in(_rk, 7), (2,), 0, max(1, 2048 // 4) + 1, jnp.int32)
        _lenS2 = 2048 - jax.random.randint(jax.random.fold_in(_rk, 8), (2,), 0, max(1, 2048 // 4) + 1, jnp.int32)
        cond_1024 = 0.00782532 + 1.00527 * jax.random.normal(jax.random.fold_in(_rk, 11), (2, 512), jnp.float32)
        return (x, cond_1024)
    x, cond_1024 = _rec_inputs()

    def _L0_cond_setup():
        import jax, jax.numpy as jnp
        import numpy as np
        INV_SQRT2 = 0.7071067811865476
        key = jax.random.key(seed)
        k1, k2, k3, k4 = jax.random.split(key, 4)
        B, N, d = (8, 2048, 512)
        scale = 1.0 / np.sqrt(d)
        return {'v': jax.random.normal(k1, (B, N, d), dtype=jnp.float32), 'q_pool': jax.random.normal(k2, (B, d), dtype=jnp.float32), 'W1': jax.random.normal(k3, (d, d), dtype=jnp.float32) * scale, 'b1': jnp.zeros((d,), dtype=jnp.float32), 'W2': jax.random.normal(k4, (d, d), dtype=jnp.float32) * scale, 'b2': jnp.zeros((d,), dtype=jnp.float32)}
    _L0_cond_all = _L0_cond_setup()
    _L0_cond_in = {k: v for k, v in _L0_cond_all.items() if k in ('W1', 'b1', 'W2', 'b2')}
    del _L0_cond_all

    def _L1_cond_setup():
        import jax, jax.numpy as jnp
        import numpy as np
        N, T, D, H = (64, 256, 512, 512)
        key = jax.random.key(seed)
        k1, k2, k3, k4 = jax.random.split(key, 4)
        x = jax.random.normal(k1, (N, T, D), dtype=jnp.float32)
        h0 = jax.random.normal(k2, (N, H), dtype=jnp.float32)
        Wx = jax.random.normal(k3, (D, H), dtype=jnp.float32) / jnp.sqrt(jnp.float32(D))
        Wh = jax.random.normal(k4, (H, H), dtype=jnp.float32) / jnp.sqrt(jnp.float32(H))
        b = jnp.zeros((H,), dtype=jnp.float32)
        return {'x': x, 'h0': h0, 'Wx': Wx, 'Wh': Wh, 'b': b}
    _L1_cond_all = _L1_cond_setup()
    _L1_cond_in = {k: v for k, v in _L1_cond_all.items() if k in ('Wx', 'Wh', 'b')}
    del _L1_cond_all

    def _L2_cond_setup():
        import jax, jax.numpy as jnp
        import numpy as np
        D_MODEL = 512
        D_FF = 2048
        N_EXPERTS = 8
        TOP_K = 2
        N_SHARED = 2
        B, T = (4, 1024)
        key = jax.random.key(seed)
        ks = jax.random.split(key, 9)
        Hs = D_FF // 2
        Hr = D_FF // 4
        inp = {'x': jax.random.normal(ks[0], (B, T, D_MODEL), dtype=jnp.float32), 't_emb': jax.random.normal(ks[1], (B, D_MODEL), dtype=jnp.float32), 'W_router': 0.01 * jax.random.normal(ks[2], (N_EXPERTS, 2 * D_MODEL), dtype=jnp.float32), 'router_bias': jnp.zeros((N_EXPERTS,), dtype=jnp.float32), 's_w1': 0.02 * jax.random.normal(ks[3], (N_SHARED, Hs, D_MODEL), dtype=jnp.float32), 's_w3': 0.02 * jax.random.normal(ks[4], (N_SHARED, Hs, D_MODEL), dtype=jnp.float32), 's_w2': 0.02 * jax.random.normal(ks[5], (N_SHARED, D_MODEL, Hs), dtype=jnp.float32), 'r_w1': 0.02 * jax.random.normal(ks[6], (N_EXPERTS, Hr, D_MODEL), dtype=jnp.float32), 'r_w2': 0.02 * jax.random.normal(ks[7], (N_EXPERTS, D_MODEL, Hr), dtype=jnp.float32)}
        return inp
    _L2_cond_all = _L2_cond_setup()
    _L2_cond_in = {k: v for k, v in _L2_cond_all.items() if k in ('W_router', 'router_bias', 's_w1', 's_w3', 's_w2', 'r_w1', 'r_w2')}
    del _L2_cond_all

    def _L3_cond_setup():
        import jax, jax.numpy as jnp
        import numpy as np
        LATENT = 512
        key = jax.random.key(seed)
        k1, k2, k3, k4 = jax.random.split(key, 4)
        B, T, D = (64, 256, LATENT)
        h_t = jax.random.normal(k1, (B, D), dtype=jnp.float32)
        z = jax.random.normal(k2, (B, T, D), dtype=jnp.float32)
        bound = 1.0 / np.sqrt(2 * D)
        W = jax.random.uniform(k3, (D, 2 * D), minval=-bound, maxval=bound, dtype=jnp.float32)
        b = jax.random.uniform(k4, (D,), minval=-bound, maxval=bound, dtype=jnp.float32)
        alpha = jnp.full((D,), 0.1, dtype=jnp.float32)
        return {'h_t': h_t, 'z': z, 'W': W, 'b': b, 'alpha': alpha}
    _L3_cond_all = _L3_cond_setup()
    _L3_cond_in = {k: v for k, v in _L3_cond_all.items() if k in ('W', 'b', 'alpha')}
    del _L3_cond_all
    return {'x': x, 'cond_1024': cond_1024, 'L0_cond_W1': _L0_cond_in['W1'], 'L0_cond_b1': _L0_cond_in['b1'], 'L0_cond_W2': _L0_cond_in['W2'], 'L0_cond_b2': _L0_cond_in['b2'], 'L1_cond_Wx': _L1_cond_in['Wx'], 'L1_cond_Wh': _L1_cond_in['Wh'], 'L1_cond_b': _L1_cond_in['b'], 'L2_cond_W_router': _L2_cond_in['W_router'], 'L2_cond_router_bias': _L2_cond_in['router_bias'], 'L2_cond_s_w1': _L2_cond_in['s_w1'], 'L2_cond_s_w3': _L2_cond_in['s_w3'], 'L2_cond_s_w2': _L2_cond_in['s_w2'], 'L2_cond_r_w1': _L2_cond_in['r_w1'], 'L2_cond_r_w2': _L2_cond_in['r_w2'], 'L3_cond_W': _L3_cond_in['W'], 'L3_cond_b': _L3_cond_in['b'], 'L3_cond_alpha': _L3_cond_in['alpha']}

def reference(x, cond_1024, L0_cond_W1, L0_cond_b1, L0_cond_W2, L0_cond_b2, L1_cond_Wx, L1_cond_Wh, L1_cond_b, L2_cond_W_router, L2_cond_router_bias, L2_cond_s_w1, L2_cond_s_w3, L2_cond_s_w2, L2_cond_r_w1, L2_cond_r_w2, L3_cond_W, L3_cond_b, L3_cond_alpha):
    import jax
    import jax.numpy as jnp

    def _L0_cond_ref(v, q_pool, W1, b1, W2, b2):
        import jax, jax.numpy as jnp
        import numpy as np
        INV_SQRT2 = 0.7071067811865476
        B, N, d = v.shape
        h = jax.nn.silu(q_pool @ W1.T + b1)
        gate = jax.nn.sigmoid(h @ W2.T + b2)[:, None, :]
        levels = int(np.log2(N))
        a = v
        details = []
        for _ in range(levels):
            e, o = (a[:, 0::2], a[:, 1::2])
            details.append((e - o) * INV_SQRT2)
            a = (e + o) * INV_SQRT2
        a = a * gate
        for dc in reversed(details):
            dc = dc * gate
            e = (a + dc) * INV_SQRT2
            o = (a - dc) * INV_SQRT2
            n = e.shape[1]
            a = jnp.stack([e, o], axis=2).reshape(B, 2 * n, d)
        return v + a

    def _L1_cond_ref(x, h0, Wx, Wh, b):
        import jax, jax.numpy as jnp
        import numpy as np
        N, T, D, H = (64, 256, 512, 512)
        xw = jnp.einsum('ntd,dh->nth', x, Wx) + b

        def step(prev_h, xw_t):
            next_h = jnp.tanh(xw_t + prev_h @ Wh)
            return (next_h, next_h)
        _, hs = jax.lax.scan(step, h0, jnp.swapaxes(xw, 0, 1))
        return jnp.swapaxes(hs, 0, 1)

    def _L2_cond_ref(x, t_emb, W_router, router_bias, s_w1, s_w3, s_w2, r_w1, r_w2):
        import jax, jax.numpy as jnp
        import numpy as np
        D_MODEL = 512
        D_FF = 2048
        N_EXPERTS = 8
        TOP_K = 2
        N_SHARED = 2
        B, T = (4, 1024)
        Bn, Tn, C = x.shape
        N = Bn * Tn
        x_flat = x.reshape(N, C)
        t_flat = jnp.broadcast_to(t_emb[:, None, :], (Bn, Tn, C)).reshape(N, C)
        shared_out = jnp.zeros_like(x_flat)
        for e in range(N_SHARED):
            h = jax.nn.silu(x_flat @ s_w1[e].T) * (x_flat @ s_w3[e].T)
            shared_out = shared_out + h @ s_w2[e].T
        shared_out = shared_out / N_SHARED
        router_in = jnp.concatenate([x_flat, t_flat], axis=-1)
        s = jax.nn.sigmoid((router_in @ W_router.T).astype(jnp.float32))
        sel_scores = s + router_bias
        _, topk_idx = jax.lax.top_k(sel_scores, TOP_K)
        s_sel = jnp.take_along_axis(s, topk_idx, axis=1)
        denom = jnp.sum(s_sel, axis=1, keepdims=True)
        gates = jnp.where(denom > 1e-09, s_sel / (denom + 1e-09), 1.0 / TOP_K).astype(x.dtype)
        gates_full = jnp.sum(jax.nn.one_hot(topk_idx, N_EXPERTS, dtype=x.dtype) * gates[..., None], axis=1)
        routed_out = jnp.zeros_like(x_flat)
        for e in range(N_EXPERTS):
            h = jax.nn.gelu(x_flat @ r_w1[e].T, approximate=False)
            routed_out = routed_out + h @ r_w2[e].T * gates_full[:, e:e + 1]
        out = (shared_out + routed_out) / (N_SHARED + TOP_K)
        return out.reshape(Bn, Tn, C)

    def _L3_cond_ref(h_t, z, W, b, alpha):
        import jax, jax.numpy as jnp
        import numpy as np
        LATENT = 512
        D = h_t.shape[-1]
        Wh = W[:, :D]
        Wz = W[:, D:]
        leak = 1.0 - alpha

        def step(h, z_t):
            gate = jax.nn.sigmoid(h @ Wh.T + z_t @ Wz.T + b)
            h_new = jnp.tanh(h * leak + gate * z_t)
            return (h_new, h_new)
        _, hs = jax.lax.scan(step, h_t, jnp.swapaxes(z, 0, 1))
        return jnp.swapaxes(hs, 0, 1)
    x = x + _L0_cond_ref(x, cond_1024, L0_cond_W1, L0_cond_b1, L0_cond_W2, L0_cond_b2)
    x = x + _L1_cond_ref(x, cond_1024, L1_cond_Wx, L1_cond_Wh, L1_cond_b)
    x = x + _L2_cond_ref(x, cond_1024, L2_cond_W_router, L2_cond_router_bias, L2_cond_s_w1, L2_cond_s_w3, L2_cond_s_w2, L2_cond_r_w1, L2_cond_r_w2)
    x = x + _L3_cond_ref(cond_1024, x, L3_cond_W, L3_cond_b, L3_cond_alpha)
    return x

_drawn_inputs = setup_inputs


def setup_inputs(seed=0):
    import zlib

    import numpy as np

    out = dict(_drawn_inputs(seed))
    spreads = {'L0_cond_b1': (0.0, 0.8),
     'L0_cond_b2': (0.0, 0.8),
     'L1_cond_b': (0.0, 0.433),
     'L2_cond_router_bias': (0.0, 2.0),
     'L3_cond_alpha': (0.10000000149011612, 0.6)}
    factors = {'L2_cond_W_router': 22.387, 'L3_cond_b': 51.287}
    for name, (base, spread) in spreads.items():
        noise = np.random.default_rng([zlib.crc32(name.encode()), seed]).standard_normal(out[name].shape)
        drawn = base * np.exp(spread * noise) if base else spread * noise
        out[name] = jnp.asarray(drawn.astype(out[name].dtype))
    for name, factor in factors.items():
        out[name] = (out[name] * factor).astype(out[name].dtype)
    return out
```

```python
from contextlib import ExitStack

import numpy as np
import concourse.bass as bass
from concourse import mybir

ALU = mybir.AluOpType
ACT = mybir.ActivationFunctionType
AX = mybir.AxisListType
F32 = mybir.dt.float32
F32R = mybir.dt.float32r
F16 = mybir.dt.float16
I32 = mybir.dt.int32

P = 128
BATCH, TIME, D = 2, 2048, 512
KD = D // P
SEGS = 32
STEPS = TIME // SEGS
LANES = SEGS * BATCH
TOKENS = BATCH * TIME
CHUNK_STEPS = 4
CW = CHUNK_STEPS * LANES
CHUNKS = TOKENS // CW
TOL = 2.0 ** -19
ROUND_BLOCK = 4

EXPERTS = 8
SHARED_UNITS = 8
GW = 512
HALVES = 2
HTOK = TOKENS // HALVES
GROUPS = HTOK // GW
HCHUNKS = CHUNKS // HALVES


def wait_alone(eng, semaphore, value, least):
    if not isinstance(value, int):
        eng.compute_val(value)
    eng.wait_ge(semaphore, least)
    eng.wait_ge(semaphore, value)


def load_x(sp, xs, x_in, x_loaded):
    with sp.Fori(0, CHUNKS) as c:
        sp.dma_start(xs[:, bass.ds(c, 1)], x_in[bass.ds(c, 1)].rearrange("o p k n -> p o k n")).then_inc(x_loaded, 16)


def setup_gate(nc, src, gate2, cond, lt, early):
    with ExitStack() as ctx:
        sb = lambda n, s, d=F32: ctx.enter_context(nc.sbuf_tensor(n, s, d))
        sem = lambda n: ctx.enter_context(nc.semaphore(n))
        w1 = sb("gate_w1", [P, KD, D])
        w2 = sb("gate_w2", [P, KD, D])
        wrt = sb("gate_wrt", [P, KD, EXPERTS])
        b12 = sb("gate_b", [P, 2, KD])
        pre = sb("gate_pre", [P, KD, BATCH])
        sig = sb("gate_sig", [P, KD, BATCH])
        hid = sb("gate_hid", [P, KD, BATCH])
        ps = [ctx.enter_context(nc.psum_tensor(f"gate_ps{i}", [P, 512], F32)) for i in range(3)]
        loaded, mm_done, pre_done = sem("gate_loaded"), sem("gate_mm_done"), sem("gate_pre_done")
        sig_done, hid_done, g_done = sem("gate_sig_done"), sem("gate_hid_done"), sem("gate_g_done")
        block = ctx.enter_context(nc.Block())

        @block.sync
        def _(sp):
            sp.dma_start(cond[:], src["cond"]).then_inc(loaded, 16)
            sp.dma_start(b12[:, 0, :], src["b1"]).then_inc(loaded, 16)
            sp.dma_start(b12[:, 1, :], src["b2"]).then_inc(loaded, 16)
            sp.dma_start(wrt[:], src["router_t"]).then_inc(loaded, 16)
            sp.dma_start(w1[:], src["w1"]).then_inc(loaded, 16)
            sp.dma_start(w2[:], src["w2"]).then_inc(loaded, 16)
            load_x(sp, early[0], src["x"], early[1])

        @block.tensor
        def _(pe):
            pe.wait_ge(loaded, 96)
            for k in range(KD):
                mm = nc.tensor.matmul(ps[2][0:EXPERTS, 0:BATCH], wrt[:, k, :], cond[:, k, :], start=(k == 0), stop=(k == KD - 1))
            for layer, (w, x) in enumerate(((w1, cond), (w2, hid))):
                if layer == 1:
                    pe.wait_ge(hid_done, 1)
                for m in range(KD):
                    for k in range(KD):
                        mm = nc.tensor.matmul(ps[layer][:, BATCH * m:BATCH * m + BATCH], w[:, k, m * P:(m + 1) * P], x[:, k, :],
                                              start=(k == 0), stop=(k == KD - 1))
                mm.then_inc(mm_done, 1)

        @block.vector
        def _(dve):
            def add_bias(layer):
                dve.wait_ge(mm_done, layer + 1)
                nc.vector.tensor_tensor(pre[:], ps[layer][:, 0:KD * BATCH].rearrange("p (m b) -> p m b", b=BATCH),
                                        b12[:, layer, :].unsqueeze(2).broadcast_to([P, KD, BATCH]), ALU.add).then_inc(pre_done, 1)
            add_bias(0)
            nc.vector.tensor_copy(lt[:], ps[2][0:EXPERTS, 0:BATCH]).then_inc(g_done, 1)
            dve.wait_ge(sig_done, 1)
            nc.vector.tensor_tensor(hid[:], pre[:], sig[:], ALU.mult).then_inc(hid_done, 1)
            dve.wait_ge(hid_done, 1)
            add_bias(1)
            dve.wait_ge(sig_done, 2)
            nc.vector.tensor_scalar(gate2[:], sig[:], 2.0, None, ALU.add).then_inc(g_done, 1)

        @block.scalar
        def _(act):
            for layer in range(2):
                act.wait_ge(pre_done, layer + 1)
                if layer == 1:
                    act.wait_ge(hid_done, 1)
                nc.scalar.activation(sig[:], pre[:], ACT.Sigmoid).then_inc(sig_done, 1)


def scan_layer(nc, name, src, x_in, x_out, cond, ident, ones, gate2, leaky, early=None):
    with ExitStack() as ctx:
        sb = lambda n, s, d=F32: ctx.enter_context(nc.sbuf_tensor(f"{name}_{n}", s, d))
        sem = lambda n: ctx.enter_context(nc.semaphore(f"{name}_{n}"))

        xs, x_loaded = early if early else (sb("xs", [P, CHUNKS, KD, CW]), sem("x_loaded"))
        wraw = sb("wraw", [P, 2, KD, D])
        wscaled = sb("wscaled", [P, KD, D])
        wr_hi, wr_lo = sb("wr_hi", [P, KD, D], F16), sb("wr_lo", [P, KD, D], F16)
        wx_hi, wx_lo = sb("wx_hi", [P, KD, D], F32R), sb("wx_lo", [P, KD, D], F32R)
        brow, bs = sb("brow", [1, D]), sb("bs", [1, D])
        b_hi, b_lo = sb("b_hi", [1, D], F32R), sb("b_lo", [1, D], F32R)
        one_f, one_r = sb("one_f", [1, CW]), sb("one_r", [1, CW], F32R)
        mx = sb("mx", [P, 4])
        scale, inv_scale = sb("scale", [P, 1]), sb("inv_scale", [P, 1])
        decay = sb("decay", [P, KD])
        x_hi = [sb(f"x_hi{i}", [P, KD, CW], F32R) for i in range(2)]
        x_lo = [sb(f"x_lo{i}", [P, KD, CW], F32R) for i in range(2)]
        hist = [sb(f"hist{i}", [P, KD, CW]) for i in range(2)]
        xo = [sb(f"xo{i}", [P, KD, CW]) for i in range(2)]
        h_hi, h_lo = sb("h_hi", [P, KD, LANES + BATCH], F16), sb("h_lo", [P, KD, LANES + BATCH], F16)
        hd = sb("hd", [P, KD, LANES + BATCH])
        gt, gz, arg = sb("gt", [P, KD, LANES]), sb("gz", [P, KD, LANES]), sb("arg", [P, KD, LANES])
        e_prev, e_diff = sb("e_prev", [P, KD, LANES - BATCH]), sb("e_diff", [P, KD, LANES - BATCH])
        running = sb("running", [1, 1], I32)
        acc = [ctx.enter_context(nc.psum_tensor(f"{name}_acc{i}", [P, KD, CW], F32)) for i in range(2)]
        pm = ctx.enter_context(nc.psum_tensor(f"{name}_pm", [P, 512], F32))

        w_in, w_mm, w_chain = sem("w_in"), sem("w_mm"), sem("w_chain")
        bulk_done = sem("bulk_done")
        summed = sem("summed")

        hi_ready, lo_ready = sem("hi_ready"), sem("lo_ready")
        h32_ready, hd_ready = sem("h32_ready"), sem("hd_ready")
        stored = [sem("stored0"), sem("stored1")]

        with nc.Block() as block:
            @block.sync
            def _(sp):
                for s in (hi_ready, lo_ready, h32_ready, hd_ready):
                    sp.sem_inc(s, 1)
                for s in stored:
                    sp.sem_inc(s, 16)
                sp.dma_start(wraw[:, 0], src["wr"]).then_inc(w_in, 16)
                sp.dma_start(wraw[:, 1], src["wx"]).then_inc(w_in, 16)
                sp.dma_start(brow[:], src["b"]).then_inc(w_in, 16)
                if leaky:
                    sp.dma_start(decay[:], src["alpha"]).then_inc(w_in, 16)
                if not early:
                    load_x(sp, xs, x_in, x_loaded)

            @block.gpsimd
            def _(pool):
                nc.gpsimd.memset(xo[0][:], 0.0).then_inc(summed, 2)
                nc.gpsimd.memset(xo[1][:], 0.0).then_inc(bulk_done, 2)

            @block.scalar
            def _(act):
                act.wait_ge(x_loaded, 16 * CHUNKS)
                if gate2 is not None:
                    for k in range(KD):
                        for b in range(BATCH):
                            xkb = xs[:, :, k, :].rearrange("p c (n b) -> p c n b", b=BATCH)[:, :, :, b]
                            nc.scalar.activation(xkb, xkb, ACT.Copy, scale=gate2[:, k, b:b + 1])

            @block.tensor
            def _(pe):
                pe.wait_ge(w_chain, 3)
                nc.tensor.matmul(pm[0:1, 0:P], mx[:, 2:3], ident[:], start=True, stop=True).then_inc(w_mm, 1)
                pe.wait_ge(w_chain, 4)
                nc.tensor.matmul(pm[:, P:P + 1], ones[:], mx[0:1, 3:4], start=True, stop=True).then_inc(w_mm, 1)

            @block.vector
            def _(dve):
                done = [0]

                def step(ins):
                    done[0] += 1
                    ins.then_inc(w_chain, 1)
                    dve.wait_ge(w_chain, done[0])

                dve.wait_ge(w_in, 64 if leaky else 48)
                step(nc.vector.tensor_reduce(mx[:, 0:1], wraw[:, 0], AX.XY, ALU.max))
                step(nc.vector.tensor_reduce(mx[:, 1:2], wraw[:, 0], AX.XY, ALU.min))
                step(nc.vector.scalar_tensor_tensor(mx[:, 2:3], mx[:, 1:2], -1.0, mx[:, 0:1], ALU.mult, ALU.max))
                dve.wait_ge(w_mm, 1)
                step(nc.vector.tensor_reduce(mx[0:1, 3:4], pm[0:1, 0:P], AX.X, ALU.max))
                dve.wait_ge(w_mm, 2)
                step(nc.vector.tensor_scalar(mx[:, 0:1], pm[:, P:P + 1], 2.0 ** -80, 2.0 ** 100, ALU.max, ALU.min))
                step(nc.vector.tensor_single_scalar(mx[:, 1:2].bitcast(I32), mx[:, 0:1].bitcast(I32), 0x7F800000, ALU.bitwise_and))
                step(nc.vector.tensor_scalar(inv_scale[:], mx[:, 1:2], 2.0 ** -13, None, ALU.mult))
                step(nc.vector.tensor_scalar(scale[:].bitcast(I32), mx[:, 1:2].bitcast(I32), -1.0, float((254 + 13) << 23), ALU.mult, ALU.add))
                step(nc.vector.tensor_scalar(wscaled[:], wraw[:, 0], scale[:, 0:1], None, ALU.mult))
                step(nc.vector.tensor_copy(wr_hi[:], wscaled[:]))
                step(nc.vector.tensor_tensor(wr_lo[:], wscaled[:], wr_hi[:], ALU.subtract))
                step(nc.vector.tensor_scalar(wscaled[:], wraw[:, 1], scale[:, 0:1], None, ALU.mult))
                step(nc.vector.tensor_copy(wx_hi[:], wscaled[:]))
                step(nc.vector.tensor_tensor(wx_lo[:], wscaled[:], wx_hi[:].bitcast(F32), ALU.subtract))
                step(nc.vector.tensor_scalar(bs[:], brow[:], scale[0:1, 0:1], None, ALU.mult))
                step(nc.vector.tensor_copy(b_hi[:], bs[:]))
                step(nc.vector.tensor_tensor(b_lo[:], bs[:], b_hi[:].bitcast(F32), ALU.subtract))
                step(nc.vector.memset(one_f[:], 1.0))
                step(nc.vector.tensor_copy(one_r[:], one_f[:]))
                step(nc.vector.memset(h_hi[:], 0.0))
                step(nc.vector.memset(h_lo[:], 0.0))
                step(nc.vector.memset(hd[:], 0.0))
                step(nc.vector.memset(e_prev[:], 0.0))
                step(nc.vector.tensor_copy(h_hi[:, :, 0:BATCH], cond[:]))
                step(nc.vector.tensor_tensor(h_lo[:, :, 0:BATCH], cond[:], h_hi[:, :, 0:BATCH], ALU.subtract))
                if leaky:
                    step(nc.vector.tensor_scalar(decay[:], decay[:], -1.0, 1.0, ALU.mult, ALU.add))
                    step(nc.vector.tensor_tensor(hd[:, :, 0:BATCH], cond[:], decay[:].unsqueeze(2).broadcast_to([P, KD, BATCH]), ALU.mult))


        x_ready = sem("x_ready")
        x_hi_ready = sem("x_hi_ready")
        pre_ready = sem("pre_ready")
        g_ready, gz_ready, arg_ready = sem("g_ready"), sem("gz_ready"), sem("arg_ready")
        check = sem("check")
        check_row = sem("check_row")
        CHECK_LINKS = 6

        def over_rounds(eng, round_program):
            with eng.register(f"{name}_{eng.engine.name}_running") as go:
                eng.reg_mov(go, 1)
                with eng.Fori(0, SEGS // ROUND_BLOCK) as rb:
                    with eng.If_ne(go, 0):
                        with eng.Fori(0, ROUND_BLOCK) as ri:
                            with eng.If_ne(go, 0):
                                r = rb * ROUND_BLOCK + ri
                                round_program(r)
                                wait_alone(eng, check, (r + 1) * CHECK_LINKS, CHECK_LINKS)
                                eng.reg_load(go, running[0:1, 0:1])

        def over_chunks(eng, r, chunk_program):
            q0, u0 = r * CHUNKS, r * (CHUNKS // 2)
            chunk_program(q0, 0, 0, u0)
            with eng.Fori(0, CHUNKS // 2 - 1) as i:
                chunk_program(q0 + i * 2 + 1, 1, i * 2 + 1, u0 + i)
                chunk_program(q0 + i * 2 + 2, 0, i * 2 + 2, u0 + i + 1)
            chunk_program(q0 + CHUNKS - 1, 1, CHUNKS - 1, u0 + CHUNKS // 2 - 1)

        with nc.Block() as block:
            @block.sync
            def _(sp):
                def store(q, p, c, use):
                    sp.wait_ge(summed, q + 3)
                    sp.dma_start(x_out[bass.ds(c, 1)].rearrange("o p k n -> p (o k) n"), xo[p][:]).then_inc(stored[p], 16)

                def one_round(r):
                    over_chunks(sp, r, store)
                    for p in range(2):
                        wait_alone(sp, stored[p], (r + 1) * (CHUNKS // 2) * 16 + 16, 16)

                over_rounds(sp, one_round)

            @block.gpsimd
            def _(pool):
                def split(q, p, c):
                    xc = xs[:, bass.ds(c, 1)].rearrange("p o k n -> p (o k) n")
                    wait_alone(pool, bulk_done, q + 1, 1)
                    nc.gpsimd.tensor_copy(x_hi[p][:], xc).then_inc(x_hi_ready, 1)
                    wait_alone(pool, x_hi_ready, q + 1, 1)
                    nc.gpsimd.tensor_tensor(x_lo[p][:], xc, x_hi[p][:].bitcast(F32), ALU.subtract).then_inc(x_ready, 1)

                def add_states(q, p, c, use):
                    xc = xs[:, bass.ds(c, 1)].rearrange("p o k n -> p (o k) n")
                    pool.wait_ge(h32_ready, (q + 1) * CHUNK_STEPS + 1)
                    wait_alone(pool, stored[p], (use + 1) * 16, 16)
                    nc.gpsimd.tensor_tensor(xo[p][:], xc, hist[p][:], ALU.add).then_inc(summed, 1)

                def chunk(q, p, c, use):
                    if not (isinstance(c, int) and c == CHUNKS - 1):
                        split(q + 1, 1 - p, c + 1)
                    if not (isinstance(c, int) and c == 0):
                        add_states(q - 1, 1 - p, c - 1, use if p else use - 1)

                def one_round(r):
                    split(r * CHUNKS, 0, 0)
                    over_chunks(pool, r, chunk)
                    add_states(r * CHUNKS + CHUNKS - 1, 1, CHUNKS - 1, (r + 1) * (CHUNKS // 2) - 1)

                over_rounds(pool, one_round)

            @block.tensor
            def _(pe):
                def bulk(q_next, p, m):
                    if m == 0:
                        pe.wait_ge(x_ready, q_next + 1)
                    cols = slice(m * P, (m + 1) * P)
                    nc.tensor.matmul(acc[p][:, m, :], b_hi[:, cols], one_r[:], start=(m % 2 == 0), stop=False, skip_group_check=True)
                    nc.tensor.matmul(acc[p][:, m, :], b_lo[:, cols], one_r[:], start=False, stop=False, skip_group_check=True)
                    for k in range(KD):
                        for w, x in ((wx_hi, x_hi), (wx_lo, x_hi), (wx_hi, x_lo)):
                            mm = nc.tensor.matmul(acc[p][:, m, :], w[:, k, cols], x[p][:, k, :], start=False, stop=False, skip_group_check=True)
                    if m == KD - 1:
                        mm.then_inc(bulk_done, 1)

                def chunk(q, p, c, use):
                    for j in range(CHUNK_STEPS):
                        s = q * CHUNK_STEPS + j
                        o = 0 if isinstance(c, int) and c == 0 and j == 0 else BATCH
                        out = [acc[p][:, m, j * LANES:(j + 1) * LANES] for m in range(KD)]
                        pe.wait_ge(hi_ready, s + 1)
                        if not leaky:
                            pe.wait_ge(h32_ready, s + 1)
                        for m in range(KD):
                            for k in range(KD):
                                for w in (wr_hi, wr_lo):
                                    nc.tensor.matmul(out[m], w[:, k, m * P:(m + 1) * P], h_hi[:, k, o:o + LANES], start=False, stop=False,
                                                     skip_group_check=True)
                        pe.wait_ge(lo_ready, s + 1)
                        for m in range(KD):
                            for k in range(KD):
                                mm = nc.tensor.matmul(out[m], wr_hi[:, k, m * P:(m + 1) * P], h_lo[:, k, o:o + LANES], start=False,
                                                      stop=(k == KD - 1), skip_group_check=True)
                        mm.then_inc(pre_ready, 1)
                        if not (isinstance(c, int) and c == CHUNKS - 1):
                            bulk(q + 1, 1 - p, j)

                def one_round(r):
                    for m in range(KD):
                        bulk(r * CHUNKS, 0, m)
                    over_chunks(pe, r, chunk)
                    pe.wait_ge(check, r * CHECK_LINKS + 4)
                    nc.tensor.matmul(pm[0:1, 0:P], mx[:, 2:3], ident[:], start=True, stop=True).then_inc(check_row, 1)

                over_rounds(pe, one_round)

            @block.scalar
            def _(act):
                def chunk(q, p, c, use):
                    for j in range(CHUNK_STEPS):
                        s = q * CHUNK_STEPS + j
                        cols = slice(j * LANES, (j + 1) * LANES)
                        pre, in_scale = acc[p][:, :, cols], inv_scale[:, 0:1]
                        act.wait_ge(pre_ready, s + 1)
                        if leaky:
                            nc.scalar.activation(gt[:], pre, ACT.Sigmoid, scale=in_scale).then_inc(g_ready, 1)
                            act.wait_ge(arg_ready, s + 1)
                            pre, in_scale = arg[:], 1.0
                        if j == 0:
                            act.wait_ge(summed, q + 1)
                        nc.scalar.activation(h_hi[:, :, BATCH:], pre, ACT.Tanh, scale=in_scale).then_inc(hi_ready, 1)
                        nc.scalar.activation(hist[p][:, :, cols], pre, ACT.Tanh, scale=in_scale).then_inc(h32_ready, 1)

                over_rounds(act, lambda r: over_chunks(act, r, chunk))

            @block.vector
            def _(dve):
                def chunk(q, p, c, use):
                    for j in range(CHUNK_STEPS):
                        s = q * CHUNK_STEPS + j
                        o = 0 if isinstance(c, int) and c == 0 and j == 0 else BATCH
                        cols = slice(j * LANES, (j + 1) * LANES)
                        if leaky:
                            z = xs[:, bass.ds(c, 1), :, cols].rearrange("p o k n -> p (o k) n")
                            dve.wait_ge(g_ready, s + 1)
                            nc.vector.tensor_tensor(gz[:], gt[:], z, ALU.mult).then_inc(gz_ready, 1)
                            dve.wait_ge(gz_ready, s + 1)
                            dve.wait_ge(hd_ready, s + 1)
                            nc.vector.tensor_tensor(arg[:], gz[:], hd[:, :, o:o + LANES], ALU.add).then_inc(arg_ready, 1)
                        dve.wait_ge(h32_ready, s + 2)
                        dve.wait_ge(hi_ready, s + 2)
                        nc.vector.tensor_tensor(h_lo[:, :, BATCH:], hist[p][:, :, cols], h_hi[:, :, BATCH:], ALU.subtract).then_inc(lo_ready, 1)
                        if leaky:
                            nc.vector.tensor_tensor(hd[:, :, BATCH:], hist[p][:, :, cols], decay[:].unsqueeze(2).broadcast_to([P, KD, LANES]),
                                                    ALU.mult).then_inc(hd_ready, 1)

                def one_round(r):
                    over_chunks(dve, r, chunk)
                    done = [0]

                    def link(ins):
                        done[0] += 1
                        ins.then_inc(check, 1)
                        dve.wait_ge(check, r * CHECK_LINKS + done[0])

                    end = hist[1][:, :, CW - LANES:CW - BATCH]
                    link(nc.vector.tensor_tensor(e_diff[:], end, e_prev[:], ALU.subtract))
                    nc.vector.tensor_copy(e_prev[:], end)
                    link(nc.vector.tensor_reduce(mx[:, 0:1], e_diff[:], AX.XY, ALU.max))
                    link(nc.vector.tensor_reduce(mx[:, 1:2], e_diff[:], AX.XY, ALU.min))
                    link(nc.vector.scalar_tensor_tensor(mx[:, 2:3], mx[:, 1:2], -1.0, mx[:, 0:1], ALU.mult, ALU.max))
                    dve.wait_ge(check_row, r + 1)
                    link(nc.vector.tensor_reduce(mx[0:1, 3:4], pm[0:1, 0:P], AX.X, ALU.max))
                    link(nc.vector.tensor_scalar(running[:], mx[0:1, 3:4], TOL, None, ALU.is_gt))

                over_rounds(dve, one_round)


def route(nc, src, x_in, gates_t, lt, ident):
    TILES = TOKENS // P
    NB = 4
    with ExitStack() as ctx:
        sb = lambda n, s, d=F32: ctx.enter_context(nc.sbuf_tensor(f"route_{n}", s, d))
        sem = lambda n: ctx.enter_context(nc.semaphore(f"route_{n}"))
        xb = [sb(f"x{i}", [P, KD, CW]) for i in range(NB)]
        w = sb("w", [P, KD, EXPERTS])
        bias = sb("bias", [P, EXPERTS])
        rank = sb("rank", [P, EXPERTS])
        logit = sb("logit", [EXPERTS, TOKENS])
        gt = sb("gt", [EXPERTS, TOKENS])
        T3 = [P, TILES, EXPERTS]
        s, sel, eq, key, one1, both, t1, g = (sb(n, T3) for n in ("s", "sel", "eq", "key", "one1", "both", "t1", "g"))
        top, den, ok, rec = (sb(n, [P, TILES]) for n in ("top", "den", "ok", "rec"))
        pl = [ctx.enter_context(nc.psum_tensor(f"route_pl{i}", [P, 512], F32)) for i in range(2)]
        pt = ctx.enter_context(nc.psum_tensor("route_pt", T3, F32))
        pg = ctx.enter_context(nc.psum_tensor("route_pg", [P, TOKENS // 2], F32))
        const_in, x_loaded = sem("const_in"), [sem(f"x_loaded{i}") for i in range(NB)]
        lmm, lcopy, tdone, sdone, chain, gmm, gcopy, out_done = (sem(n) for n in (
            "lmm", "lcopy", "tdone", "sdone", "chain", "gmm", "gcopy", "out_done"))
        CHAIN = 23
        block = ctx.enter_context(nc.Block())

        @block.sync
        def _(sp):
            sp.dma_start(w[:], src["router_x"]).then_inc(const_in, 16)
            sp.dma_start(bias[:], src["router_bias"].partition_broadcast(P)).then_inc(const_in, 16)
            sp.dma_start(rank[:], src["rank"]).then_inc(const_in, 16)
            for i in range(NB):
                sp.dma_start(xb[i][:], x_in[i]).then_inc(x_loaded[i], 16)
            with sp.Fori(1, CHUNKS // NB) as it:
                for i in range(NB):
                    sp.wait_ge(lmm, it * NB + i - NB + 1)
                    sp.dma_start(xb[i][:], x_in[bass.ds(it * NB + i, 1)].rearrange("o p k n -> p (o k) n")).then_inc(x_loaded[i], 16)
            sp.wait_ge(gcopy, 2)
            sp.dma_start(gates_t, gt[:]).then_inc(out_done, 16)
            sp.wait_ge(out_done, 16)

        @block.tensor
        def _(pe):
            pe.wait_ge(const_in, 48)
            with pe.Fori(0, CHUNKS // NB) as it:
                for i in range(NB):
                    pe.wait_ge(x_loaded[i], (it + 1) * 16)
                    pe.wait_ge(lcopy, it * NB + i + 1)
                    for k in range(KD):
                        mm = nc.tensor.matmul(pl[i % 2][0:EXPERTS, 0:CW], w[:, k, :], xb[i][:, k, :], start=(k == 0), stop=(k == KD - 1))
                    mm.then_inc(lmm, 1)
            pe.wait_ge(lcopy, CHUNKS + 2)
            for t in range(TILES):
                mm = nc.tensor.matmul(pt[:, t, :], logit[:, t * P:(t + 1) * P], ident[0:EXPERTS, 0:EXPERTS], start=True, stop=True)
            mm.then_inc(tdone, 1)
            pe.wait_ge(chain, CHAIN)
            for half in range(2):
                pe.wait_ge(gcopy, half)
                for t in range(TILES // 2):
                    mm = nc.tensor.matmul(pg[0:EXPERTS, t * P:(t + 1) * P], g[:, half * (TILES // 2) + t, :], ident[:], start=True, stop=True)
                mm.then_inc(gmm, 1)

        @block.scalar
        def _(act):
            act.wait_ge(tdone, 1)
            nc.scalar.activation(s[:], pt[:], ACT.Sigmoid).then_inc(sdone, 1)

        @block.vector
        def _(dve):
            nc.vector.memset(top[:], 0.0).then_inc(lcopy, 2)
            with dve.Fori(0, CHUNKS // 2) as it:
                for i in range(2):
                    dve.wait_ge(lmm, it * 2 + i + 1)
                    nc.vector.tensor_tensor(
                        logit[:, bass.ds((it * 2 + i) * CW, CW)].rearrange("e (n b) -> e n b", b=BATCH),
                        pl[i][0:EXPERTS, 0:CW].rearrange("e (n b) -> e n b", b=BATCH),
                        lt[:].unsqueeze(1).broadcast_to([EXPERTS, CW // BATCH, BATCH]), ALU.add).then_inc(lcopy, 1)
            done = [0]

            def link(ins):
                done[0] += 1
                ins.then_inc(chain, 1)
                dve.wait_ge(chain, done[0])

            wide = lambda a: a.unsqueeze(2).broadcast_to(T3)
            every = lambda a: a.unsqueeze(1).broadcast_to(T3)
            dve.wait_ge(sdone, 1)
            link(nc.vector.tensor_tensor(sel[:], s[:], every(bias[:]), ALU.add))
            for turn in range(2):
                one = one1 if turn == 0 else t1
                link(nc.vector.tensor_reduce(top[:], sel[:], AX.X, ALU.max))
                link(nc.vector.tensor_tensor(eq[:], sel[:], wide(top[:]), ALU.is_equal))
                link(nc.vector.tensor_tensor(key[:], eq[:], every(rank[:]), ALU.mult))
                link(nc.vector.tensor_reduce(top[:], key[:], AX.X, ALU.max))
                link(nc.vector.tensor_tensor(one[:], key[:], wide(top[:]), ALU.is_equal))
                if turn == 0:
                    link(nc.vector.scalar_tensor_tensor(sel[:], one1[:], -1e30, sel[:], ALU.mult, ALU.add))
            link(nc.vector.tensor_tensor(both[:], one1[:], t1[:], ALU.add))
            link(nc.vector.tensor_tensor(g[:], s[:], both[:], ALU.mult))
            link(nc.vector.tensor_reduce(den[:], g[:], AX.X, ALU.add))
            link(nc.vector.tensor_scalar(ok[:], den[:], 1e-9, None, ALU.is_gt))
            link(nc.vector.tensor_scalar(rec[:], den[:], 1e-9, None, ALU.add))
            link(nc.vector.reciprocal(rec[:], rec[:]))
            link(nc.vector.scalar_tensor_tensor(rec[:], rec[:], 0.25, ok[:], ALU.mult, ALU.mult))
            link(nc.vector.tensor_scalar(ok[:], ok[:], -0.125, 0.125, ALU.mult, ALU.add))
            link(nc.vector.tensor_tensor(g[:], g[:], wide(rec[:]), ALU.mult))
            link(nc.vector.tensor_tensor(both[:], both[:], wide(ok[:]), ALU.mult))
            nc.vector.tensor_tensor(g[:], g[:], both[:], ALU.add).then_inc(chain, 1)
            assert done[0] == CHAIN - 1
            for half in range(2):
                dve.wait_ge(gmm, half + 1)
                nc.vector.tensor_copy(gt[:, half * (TOKENS // 2):(half + 1) * (TOKENS // 2)], pg[0:EXPERTS, :]).then_inc(gcopy, 1)


def experts(nc, src, x_in, x_out, gates_t):
    with ExitStack() as ctx:
        sb = lambda n, s, d=F32: ctx.enter_context(nc.sbuf_tensor(f"moe_{n}", s, d))
        sem = lambda n: ctx.enter_context(nc.semaphore(f"moe_{n}"))
        W4 = [P, KD, D]
        stage = sb("stage", W4)
        a_hi, a_lo = [sb(f"a_hi{i}", W4, F32R) for i in range(2)], [sb(f"a_lo{i}", W4, F32R) for i in range(2)]
        b_hi, b_lo = [sb(f"b_hi{i}", W4, F32R) for i in range(2)], [sb(f"b_lo{i}", W4, F32R) for i in range(2)]
        x_hi, x_lo = sb("x_hi", [P, HCHUNKS, KD, CW], F32R), sb("x_lo", [P, HCHUNKS, KD, CW], F32R)
        acc = sb("acc", [P, HCHUNKS, KD, CW])
        h_hi, h_lo = sb("h_hi", [P, 6, GW], F32R), sb("h_lo", [P, 6, GW], F32R)
        curve = [sb(f"curve{i}", [P, GW]) for i in range(2)]
        hb = [sb(f"hb{i}", [P, GW]) for i in range(2)]
        gb = [sb(f"gb{i}", [P, GW]) for i in range(2)]
        p1 = [ctx.enter_context(nc.psum_tensor(f"moe_p1_{i}", [P, GW], F32)) for i in range(4)]
        p2 = [ctx.enter_context(nc.psum_tensor(f"moe_p2_{i}", [P, GW], F32)) for i in range(4)]

        stage_in, stage_hi, stage_free = sem("stage_in"), sem("stage_hi"), sem("stage_free")
        a_ready, b_ready, unit_done = sem("a_ready"), sem("b_ready"), sem("unit_done")
        x_loaded = [sem("x_loaded0"), sem("x_loaded1")]
        xh_ready, xl_ready, stored = sem("xh_ready"), sem("xl_ready"), sem("stored")
        filled = [sem(f"filled{m}") for m in range(4)]
        emptied = [sem(f"emptied{m}") for m in range(4)]
        curve_ready = [sem(f"curve_ready{m}") for m in range(2)]
        h_ready = [sem(f"h_ready{m}") for m in range(4)]
        hh_ready = [sem(f"hh_ready{m}") for m in range(4)]
        hl_ready = [sem(f"hl_ready{m}") for m in range(4)]
        used = [sem(f"used{m}") for m in range(4)]
        added = sem("added")
        gates_in = [sem("gates_in0"), sem("gates_in1")]

        with nc.Block() as block:
            @block.sync
            def _(sp):
                for s in (*emptied, *h_ready, *used, added, stage_free):
                    sp.sem_inc(s, 1)
                sp.sem_inc(unit_done, 2)

        ITER = 4
        UNITS = 16
        KINDS = (False, True)

        def numbers(hf, routed, it, j):
            v = hf * UNITS + (8 if routed else 0) + it * 2 + j // GROUPS
            n = hf * (UNITS * GROUPS) + (32 if routed else 0) + it * 8 + j
            r = hf * 32 + it * 8 + j
            return v, n, r, lambda m: n if m < 2 else r

        def slot(j, m):
            return m + 4 if j % 2 and m < 2 else m

        def tiles(routed):
            return 4 if routed else 2

        with nc.Block() as block:
            @block.sync
            def _(sp):
                with sp.Fori(0, HALVES) as hf:
                    for routed in KINDS:
                        with sp.Fori(0, 8) as u:
                            v = hf * UNITS + (8 if routed else 0) + u
                            sp.wait_ge(stage_free, v * 2 + 1)
                            sp.dma_start(stage[:], src["routed_a" if routed else "shared_a"][bass.ds(u, 1)].rearrange("o p k n -> p (o k) n")).then_inc(stage_in, 16)
                            sp.wait_ge(stage_free, v * 2 + 2)
                            sp.dma_start(stage[:, 0:tiles(routed)], src["routed_b" if routed else "shared_b"][bass.ds(u, 1)].rearrange("o p k n -> p (o k) n")).then_inc(stage_in, 16)

            @block.gpsimd
            def _(pool):
                with pool.Fori(0, HALVES) as hf:
                    for routed in KINDS:
                        with pool.Fori(0, ITER) as it:
                            for up in range(2):
                                v, _, _, _ = numbers(hf, routed, it, up * GROUPS)
                                pool.wait_ge(unit_done, v + 1)
                                for n, (hi, lo, kt, ready) in enumerate(((a_hi[up], a_lo[up], KD, a_ready), (b_hi[up], b_lo[up], tiles(routed), b_ready))):
                                    wait_alone(pool, stage_in, (v * 2 + n + 1) * 16, 16)
                                    nc.gpsimd.tensor_copy(hi[:, 0:kt], stage[:, 0:kt]).then_inc(stage_hi, 1)
                                    pool.wait_ge(stage_hi, v * 2 + n + 1)
                                    nc.gpsimd.tensor_tensor(lo[:, 0:kt], stage[:, 0:kt], hi[:, 0:kt].bitcast(F32), ALU.subtract).then_inc(ready, 1)
                                    pool.wait_ge(ready, v + 1)
                                    pool.sem_inc(stage_free, 1)

            @block.tensor
            def _(pe):
                def first(hf, routed, it, j):
                    v, n, _, _ = numbers(hf, routed, it, j)
                    g, up = j % GROUPS, j // GROUPS
                    if g == 0:
                        pe.wait_ge(a_ready, v + 1)
                    for m in range(4):
                        pe.wait_ge(emptied[m], n + 1)
                        i = 0
                        for k in range(KD):
                            for w, x in ((a_hi, x_hi), (a_lo, x_hi), (a_hi, x_lo)):
                                mm = nc.tensor.matmul(p1[m][:], w[up][:, k, m * P:(m + 1) * P], x[:, 2 * g:2 * g + 2, k, :],
                                                      start=(i == 0), stop=(i == 3 * KD - 1))
                                i += 1
                        mm.then_inc(filled[m], 1)

                def second(hf, routed, it, j):
                    v, n, r, use = numbers(hf, routed, it, j)
                    g, up = j % GROUPS, j // GROUPS
                    if g == 0:
                        pe.wait_ge(b_ready, v + 1)
                    pe.wait_ge(added, n + 1)
                    order = (2, 3, 0, 1) if routed else (0, 1)
                    for k in order:
                        pe.wait_ge(hl_ready[k], use(k) + 1)
                        for m in range(4):
                            for i, (w, h) in enumerate(((b_hi, h_hi), (b_lo, h_hi), (b_hi, h_lo))):
                                mm = nc.tensor.matmul(p2[m][:], w[up][:, k, m * P:(m + 1) * P], h[:, slot(j, k), :],
                                                      start=(k == order[0] and i == 0), stop=(k == order[-1] and i == 2))
                        mm.then_inc(used[k], 1)

                with pe.Fori(0, HALVES) as hf:
                    wait_alone(pe, xl_ready, (hf + 1) * HCHUNKS, HCHUNKS)
                    for routed in KINDS:
                        with pe.Fori(0, ITER) as it:
                            for j in range(8):
                                first(hf, routed, it, j)
                                if j:
                                    second(hf, routed, it, j - 1)
                            second(hf, routed, it, 7)

            @block.scalar
            def _(act):
                def gates(hf, it, j):
                    e = it * 2 + j // GROUPS
                    act.dma_start(gb[j % 2][:], gates_t[bass.ds(e, 1), bass.ds(hf * HTOK + (j % GROUPS) * GW, GW)].broadcast_to([P, GW])).then_inc(gates_in[j % 2], 16)

                def item(hf, routed, it, j):
                    v, n, r, use = numbers(hf, routed, it, j)
                    nt = tiles(routed)
                    if routed and j < 7:
                        gates(hf, it, j + 1)

                    def high(m):
                        if routed:
                            act.wait_ge(h_ready[m], r + 2)
                        else:
                            act.wait_ge(emptied[m + 2], n + 2)
                        if m >= 2:
                            act.wait_ge(used[m], use(m) + 1)
                        nc.scalar.copy(h_hi[:, slot(j, m), :], hb[m % 2][:]).then_inc(hh_ready[m], 1)

                    for m in range(nt):
                        act.wait_ge(filled[m], n + 1)
                        if m < 2:
                            act.wait_ge(emptied[3], n + 1)
                            if routed:
                                act.wait_ge(h_ready[3], r + 1)
                        else:
                            act.wait_ge(h_ready[m - 2], r + 2)
                        if routed:
                            nc.scalar.activation(curve[m % 2][:], p1[m][:], ACT.Gelu).then_inc(emptied[m], 1)
                        else:
                            nc.scalar.activation(curve[m % 2][:], p1[m][:], ACT.Sigmoid).then_inc(curve_ready[m], 1)
                        if m:
                            high(m - 1)
                    high(nt - 1)

                with act.Fori(0, HALVES) as hf:
                    for i in range(2):
                        act.dma_start(acc[:, 4 * i:4 * i + 4], x_in[bass.ds(hf * HCHUNKS + 4 * i, 4)].rearrange("c p k n -> p c k n")).then_inc(x_loaded[i], 16)
                    for c in range(HCHUNKS):
                        if c % 4 == 0:
                            act.wait_ge(x_loaded[c // 4], (hf + 1) * 16)
                        nc.scalar.copy(x_hi[:, c], acc[:, c]).then_inc(xh_ready, 1)
                    for routed in KINDS:
                        with act.Fori(0, ITER) as it:
                            if routed:
                                gates(hf, it, 0)
                            for j in range(8):
                                item(hf, routed, it, j)
                    act.wait_ge(added, (hf + 1) * UNITS * GROUPS + 1)
                    act.dma_start(x_out[bass.ds(hf * HCHUNKS, HCHUNKS)].rearrange("c p k n -> p c k n"), acc[:]).then_inc(stored, 16)
                    act.wait_ge(stored, (hf + 1) * 16)

            @block.vector
            def _(dve):
                def item(hf, routed, it, j):
                    v, n, r, use = numbers(hf, routed, it, j)
                    nt = tiles(routed)

                    def low(m):
                        dve.wait_ge(hh_ready[m], use(m) + 1)
                        nc.vector.tensor_tensor(h_lo[:, slot(j, m), :], hb[m % 2][:], h_hi[:, slot(j, m), :].bitcast(F32), ALU.subtract).then_inc(hl_ready[m], 1)

                    for m in range(nt):
                        if not routed:
                            dve.wait_ge(curve_ready[m], hf * 32 + it * 8 + j + 1)
                            dve.wait_ge(filled[m], n + 1)
                            nc.vector.scalar_tensor_tensor(hb[m % 2][:], curve[m % 2][:], 0.125, p1[m][:], ALU.mult, ALU.mult).then_inc(emptied[m], 1)
                        if m:
                            low(m - 1)
                        dve.wait_ge(emptied[m], n + 2)
                        if routed:
                            if m == 0:
                                dve.wait_ge(gates_in[j % 2], (hf * 16 + it * 4 + j // 2 + 1) * 16)
                            nc.vector.tensor_tensor(hb[m % 2][:], curve[m % 2][:], gb[j % 2][:], ALU.mult).then_inc(h_ready[m], 1)
                        else:
                            dve.wait_ge(filled[m + 2], n + 1)
                            nc.vector.tensor_tensor(hb[m % 2][:], hb[m % 2][:], p1[m + 2][:], ALU.mult).then_inc(emptied[m + 2], 1)
                    low(nt - 1)

                def add(hf, routed, it, j):
                    v, n, r, use = numbers(hf, routed, it, j)
                    g = j % GROUPS
                    dve.wait_ge(used[1], n + 2)
                    for m in range(4):
                        a = acc[:, 2 * g:2 * g + 2, m, :]
                        ins = nc.vector.tensor_tensor(a, a, p2[m][:].rearrange("p (c n) -> p c n", c=2), ALU.add)
                        if m == 0 and g == GROUPS - 1:
                            ins.then_inc(unit_done, 1)
                    ins.then_inc(added, 1)

                with dve.Fori(0, HALVES) as hf:
                    for c in range(HCHUNKS):
                        dve.wait_ge(xh_ready, hf * HCHUNKS + c + 1)
                        nc.vector.tensor_tensor(x_lo[:, c], acc[:, c], x_hi[:, c].bitcast(F32), ALU.subtract).then_inc(xl_ready, 1)
                    for routed in KINDS:
                        with dve.Fori(0, ITER) as it:
                            for j in range(8):
                                item(hf, routed, it, j)
                                if j:
                                    add(hf, routed, it, j - 1)
                            add(hf, routed, it, 7)


def build(nc, src, out, x2, x3, gates_t):
    with ExitStack() as ctx:
        sb = lambda n, s, d=F32: ctx.enter_context(nc.sbuf_tensor(n, s, d))
        ident, ones = sb("ident", [P, P]), sb("ones", [1, P])
        cond, gate2, lt = sb("cond", [P, KD, BATCH]), sb("gate2", [P, KD, BATCH]), sb("lt", [EXPERTS, BATCH])
        const_in = ctx.enter_context(nc.semaphore("const_in"))
        with nc.Block() as block:
            @block.sync
            def _(sp):
                sp.dma_start(ident[:], src["ident"]).then_inc(const_in, 16)
                sp.dma_start(ones[:], src["ones"]).then_inc(const_in, 16)
                sp.wait_ge(const_in, 32)
        l1 = {"wx": src["l1_wx"], "wr": src["l1_wr"], "b": src["l1_b"]}
        l3 = {"wx": src["l3_wx"], "wr": src["l3_wr"], "b": src["l3_b"], "alpha": src["l3_alpha"]}
        with ExitStack() as first:
            early = (first.enter_context(nc.sbuf_tensor("rnn_xs", [P, CHUNKS, KD, CW], F32)), first.enter_context(nc.semaphore("rnn_x_loaded")))
            setup_gate(nc, src, gate2, cond, lt, early)
            scan_layer(nc, "rnn", l1, src["x"], x2, cond, ident, ones, gate2, False, early)
        route(nc, src, x2, gates_t, lt, ident)
        experts(nc, src, x2, x3, gates_t)
        scan_layer(nc, "leaky", l3, x3, out, cond, ident, ones, None, True)


def layout(inputs):
    a = {k: np.asarray(v) for k, v in inputs.items()}

    def rows(w):
        return np.ascontiguousarray(w.reshape(-1, P, w.shape[-1]).transpose(1, 0, 2))

    def column(v):
        return np.ascontiguousarray(v.reshape(KD, P).T)

    x = a["x"].reshape(BATCH, SEGS, CHUNKS, CHUNK_STEPS, KD, P).transpose(2, 5, 4, 3, 1, 0).reshape(CHUNKS, P, KD, CW)
    w3 = a["L3_cond_W"]
    wr = a["L2_cond_W_router"]
    q = D // 2
    s1, s3 = (a[f"L2_cond_s_{n}"].reshape(SHARED_UNITS, q, D).transpose(0, 2, 1) for n in ("w1", "w3"))
    sa = np.concatenate([s1, s3], axis=2)
    s2 = a["L2_cond_s_w2"].transpose(0, 2, 1).reshape(SHARED_UNITS, q, D)
    cut = lambda w: np.ascontiguousarray(w.reshape(w.shape[0], -1, P, w.shape[-1]).transpose(0, 2, 1, 3))
    return {
        "x": np.ascontiguousarray(x),
        "cond": np.ascontiguousarray(a["cond_1024"].T.reshape(KD, P, BATCH).transpose(1, 0, 2)),
        "w1": rows(a["L0_cond_W1"].T), "b1": column(a["L0_cond_b1"]),
        "w2": rows(a["L0_cond_W2"].T), "b2": column(a["L0_cond_b2"]),
        "l1_wx": rows(a["L1_cond_Wx"]), "l1_wr": rows(a["L1_cond_Wh"]), "l1_b": a["L1_cond_b"].reshape(1, D),
        "l3_wr": rows(w3[:, :D].T), "l3_wx": rows(w3[:, D:].T), "l3_b": a["L3_cond_b"].reshape(1, D),
        "l3_alpha": column(a["L3_cond_alpha"]),
        "router_x": rows(wr[:, :D].T), "router_t": rows(wr[:, D:].T), "router_bias": a["L2_cond_router_bias"],
        "shared_a": cut(sa), "shared_b": cut(s2),
        "routed_a": cut(a["L2_cond_r_w1"].transpose(0, 2, 1)), "routed_b": cut(a["L2_cond_r_w2"].transpose(0, 2, 1)),
        "ident": np.eye(P, dtype=np.float32), "ones": np.ones((1, P), np.float32),
        "rank": np.tile(np.arange(EXPERTS, 0, -1, dtype=np.float32), (P, 1)),
    }


def restore(y):
    return np.ascontiguousarray(
        y.reshape(CHUNKS, P, KD, CHUNK_STEPS, SEGS, BATCH).transpose(5, 4, 0, 3, 2, 1).reshape(BATCH, TIME, D))


def declare(nc, arrays):
    from concourse import mybir as _mybir
    src = {n: nc.dram_tensor(f"in_{n}", a.shape, _mybir.dt.from_np(a.dtype), kind="ExternalInput").ap() for n, a in arrays.items()}
    shape = (CHUNKS, P, KD, CW)
    out = nc.dram_tensor("out_0", shape, F32, kind="ExternalOutput").ap()
    x2 = nc.dram_tensor("x2", shape, F32, kind="Internal").ap()
    x3 = nc.dram_tensor("x3", shape, F32, kind="Internal").ap()
    gates_t = nc.dram_tensor("gates_t", (EXPERTS, TOKENS), F32, kind="Internal").ap()
    return src, out, x2, x3, gates_t


def kernel(**inputs):
    import concourse.bacc as _bacc
    from concourse.bass_utils import run_bass_kernel_spmd as _run

    nc = _bacc.Bacc("TRN2", target_bir_lowering=False, num_devices=1)
    arrays = layout(inputs)
    build(nc, *declare(nc, arrays))
    r = _run(nc, [{f"in_{n}": a for n, a in arrays.items()}], core_ids=[0])
    return restore(r.results[0]["out_0"])
```
